# Optimizing a Trainium2 kernel written in Bass

```python
import numpy as np
import jax
import jax.numpy as jnp

def _softmax(x, axis=-1):
    return jax.nn.softmax(x, axis=axis)

def _gelu(x):
    return jax.nn.gelu(x, approximate=True)

def _silu(x):
    return jax.nn.silu(x)

def _sigmoid(x):
    return jax.nn.sigmoid(x)

def _layernorm(x, axis=-1, eps=1e-05):
    m = jnp.mean(x, axis=axis, keepdims=True)
    v = jnp.var(x, axis=axis, keepdims=True)
    return (x - m) / jnp.sqrt(v + eps)

def _scatter_add(tgt, idx, src, axis=0):
    return tgt.at[idx].add(src)

def _segment_sum(src, seg, n):
    return jax.ops.segment_sum(src, seg, n)
kernel_name = 'mk_conv_seq_d1_conv_nchw256_r2_2ba782'

def setup_inputs(seed: int=0):
    np.random.seed(seed)
    _w = jnp.asarray

    def _rec_inputs():
        import jax
        import jax.numpy as jnp
        _gk = jax.random.key(seed)
        x = -0.0002928 + 1 * jax.random.normal(jax.random.fold_in(_gk, 1), (4, 128, 32, 32), jnp.float32)
        return x
    x = _rec_inputs()

    def _L0_conv_setup():
        import jax, jax.numpy as jnp
        import numpy as np
        GN_GROUPS = 8
        GN_EPS = 1e-05

        def _group_norm(x, w, b):
            B, C, H, W = x.shape
            g = x.reshape(B, GN_GROUPS, C // GN_GROUPS, H * W)
            mean = g.mean(axis=(2, 3), keepdims=True)
            var = g.var(axis=(2, 3), keepdims=True)
            g = (g - mean) * jax.lax.rsqrt(var + GN_EPS)
            h = g.reshape(B, C, H * W)
            return h * w[None, :, None] + b[None, :, None]
        key = jax.random.key(seed)
        ks = jax.random.split(key, 11)
        B, C, H, W = (4, 128, 32, 32)
        s = 1.0 / np.sqrt(C)
        inp = {'x': jax.random.normal(ks[0], (B, C, H, W), dtype=jnp.float32), 'gn_w': jnp.ones((C,), jnp.float32), 'gn_b': jnp.zeros((C,), jnp.float32), 'qw': jax.random.normal(ks[1], (C, C), jnp.float32) * s, 'qb': jnp.zeros((C,), jnp.float32), 'kw': jax.random.normal(ks[2], (C, C), jnp.float32) * s, 'kb': jnp.zeros((C,), jnp.float32), 'vw': jax.random.normal(ks[3], (C, C), jnp.float32) * s, 'vb': jnp.zeros((C,), jnp.float32), 'pw': jax.random.normal(ks[4], (C, C), jnp.float32) * s, 'pb': jnp.zeros((C,), jnp.float32)}
        return inp
    _L0_conv_all = _L0_conv_setup()
    _L0_conv_in = {k: v for k, v in _L0_conv_all.items() if k in ('gn_w', 'gn_b', 'qw', 'qb', 'kw', 'kb', 'vw', 'vb', 'pw', 'pb')}
    del _L0_conv_all
    return {'x': x, 'L0_conv_gn_w': _L0_conv_in['gn_w'], 'L0_conv_gn_b': _L0_conv_in['gn_b'], 'L0_conv_qw': _L0_conv_in['qw'], 'L0_conv_qb': _L0_conv_in['qb'], 'L0_conv_kw': _L0_conv_in['kw'], 'L0_conv_kb': _L0_conv_in['kb'], 'L0_conv_vw': _L0_conv_in['vw'], 'L0_conv_vb': _L0_conv_in['vb'], 'L0_conv_pw': _L0_conv_in['pw'], 'L0_conv_pb': _L0_conv_in['pb']}

def reference(x, L0_conv_gn_w, L0_conv_gn_b, L0_conv_qw, L0_conv_qb, L0_conv_kw, L0_conv_kb, L0_conv_vw, L0_conv_vb, L0_conv_pw, L0_conv_pb):
    import jax
    import jax.numpy as jnp

    def _L0_conv_ref(x, gn_w, gn_b, qw, qb, kw, kb, vw, vb, pw, pb):
        import jax, jax.numpy as jnp
        import numpy as np
        GN_GROUPS = 8
        GN_EPS = 1e-05

        def _group_norm(x, w, b):
            B, C, H, W = x.shape
            g = x.reshape(B, GN_GROUPS, C // GN_GROUPS, H * W)
            mean = g.mean(axis=(2, 3), keepdims=True)
            var = g.var(axis=(2, 3), keepdims=True)
            g = (g - mean) * jax.lax.rsqrt(var + GN_EPS)
            h = g.reshape(B, C, H * W)
            return h * w[None, :, None] + b[None, :, None]
        B, C, H, W = x.shape
        h = _group_norm(x, gn_w, gn_b)
        q = jnp.einsum('oc,bcn->bon', qw, h) + qb[None, :, None]
        k = jnp.einsum('oc,bcn->bon', kw, h) + kb[None, :, None]
        v = jnp.einsum('oc,bcn->bon', vw, h) + vb[None, :, None]
        attn = jnp.einsum('bcn,bcm->bnm', q, k) / jnp.sqrt(jnp.asarray(C, x.dtype))
        attn = jax.nn.softmax(attn, axis=-1)
        out = jnp.einsum('bnm,bcm->bcn', attn, v)
        out = jnp.einsum('oc,bcn->bon', pw, out) + pb[None, :, None]
        return x + out.reshape(B, C, H, W)

    def _gn(v, G=32, eps=1e-05):
        B_, C_, H_, W_ = v.shape
        g = v.reshape(B_, G, C_ // G, H_, W_)
        m = jnp.mean(g, axis=(2, 3, 4), keepdims=True)
        s = jnp.var(g, axis=(2, 3, 4), keepdims=True)
        return ((g - m) / jnp.sqrt(s + eps)).reshape(v.shape)

    def _ln_c(v, eps=1e-06):
        m = jnp.mean(v, axis=1, keepdims=True)
        s = jnp.var(v, axis=1, keepdims=True)
        return (v - m) / jnp.sqrt(s + eps)

    def _ln_t(v, eps=1e-05):
        m = jnp.mean(v, axis=-1, keepdims=True)
        s = jnp.var(v, axis=-1, keepdims=True)
        return (v - m) / jnp.sqrt(s + eps)

    def _to_tokens(v):
        B_, C_, H_, W_ = v.shape
        return v.reshape(B_, C_, H_ * W_).transpose(0, 2, 1)

    def _from_tokens(t, like):
        B_, C_, H_, W_ = like.shape
        return t.transpose(0, 2, 1).reshape(B_, C_, H_, W_)
    x = _L0_conv_ref(x, L0_conv_gn_w, L0_conv_gn_b, L0_conv_qw, L0_conv_qb, L0_conv_kw, L0_conv_kb, L0_conv_vw, L0_conv_vb, L0_conv_pw, L0_conv_pb)
    return x

_drawn_inputs = setup_inputs


def setup_inputs(seed=0):
    import zlib

    import numpy as np

    out = dict(_drawn_inputs(seed))
    spreads = {'L0_conv_gn_w': (1.0, 0.2),
     'L0_conv_gn_b': (0.0, 0.1),
     'L0_conv_qb': (0.0, 0.734),
     'L0_conv_kb': (0.0, 0.8),
     'L0_conv_vb': (0.0, 0.1),
     'L0_conv_pb': (0.0, 0.1)}
    factors = {}
    for name, (base, spread) in spreads.items():
        noise = np.random.default_rng([zlib.crc32(name.encode()), seed]).standard_normal(out[name].shape)
        drawn = base * np.exp(spread * noise) if base else spread * noise
        out[name] = jnp.asarray(drawn.astype(out[name].dtype))
    for name, factor in factors.items():
        out[name] = (out[name] * factor).astype(out[name].dtype)
    return out
```

```python
from contextlib import ExitStack

import concourse.bass as bass
from concourse import mybir
from concourse.alu_op_type import AluOpType as ALU

F32 = mybir.dt.float32
F32R = mybir.dt.float32r
ACT = mybir.ActivationFunctionType
AX = mybir.AxisListType

P = 128
Q = 32
NQ = P // Q
GROUPS = 8
EPS = 1e-5
BANK = 512
LAG = 12
AHEAD = 2
V_STEP = LAG - 10
RING = 3


def build(nc, x, gn_w, gn_b, qw, qb, kw, kb, vw, vb, pw, pb, out):
    B, C, N = x.shape
    CH = N // P
    KT = CH
    CQ = CH * Q
    HALVES = N // BANK
    PT = KT // 2
    GC = BANK // P
    VP = 4
    VT = KT // VP
    SCALE = float(C) ** -0.5
    CPG = C // GROUPS
    STEPS = B * CH
    assert C == P and HALVES == 2 and 2 * NQ == CH and 2 * CQ == BANK and CQ * PT == N

    with ExitStack() as ctx:
        def sb(name, shape, dt=F32):
            return ctx.enter_context(nc.sbuf_tensor(name, shape, dt))

        def psum(name, shape):
            return ctx.enter_context(nc.psum_tensor(name, shape, F32))

        def sem(name):
            return ctx.enter_context(nc.semaphore(name))

        x_sb = sb("x_sb", [P, B, N])
        w_nat = sb("w_nat", [P, 4, P])
        rows = sb("rows", [6, P])
        cols = sb("cols", [P, 6])
        GNW, GNB, QB, KB, VB, PB = range(6)
        qb_scaled = sb("qb_scaled", [P, 1])
        out_bias = sb("out_bias", [P, 1])
        ident = sb("ident", [P, P])
        group_mean = sb("group_mean", [P, P])
        minus_half = sb("minus_half", [P, 1])
        warm = sb("warm", [P, 1])
        wqk_hi = sb("wqk_hi", [P, 2, P], F32R)
        wqk_lo = sb("wqk_lo", [P, 2, P], F32R)
        pwT = sb("pwT", [P, P])
        wpv = sb("wpv", [P, P])
        bn = sb("bn", [P, HALVES, 6])
        chan = sb("chan", [P, 2])
        gmean = sb("gmean", [P, 1])
        dmean = sb("dmean", [P, 1])
        cvar = sb("cvar", [P, 1])
        gvar = sb("gvar", [P, 1])
        rstd = sb("rstd", [P, 1])
        gscale = sb("gscale", [P, 1])
        gms = sb("gms", [P, 1])
        gshift = sb("gshift", [P, 1])
        h = sb("h", [P, 2, N])
        h_hi = sb("h_hi", [P, N], F32R)
        h_lo = sb("h_lo", [P, N], F32R)
        qk_hi = sb("qk_hi", [P, 2, N], F32R)
        qk_lo = sb("qk_lo", [P, 2, N], F32R)
        v_hi = sb("v_hi", [P, 2, KT, P], F32R)
        v_lo = sb("v_lo", [P, 2, KT, P], F32R)
        negmax = sb("negmax", [P, CH])
        den = sb("den", [P, CH])
        rden = sb("rden", [P, 2, CH])
        probs = sb("probs", [P, 2, N])
        blocks = sb("blocks", [P, 2, NQ, KT, CH, Q])
        pT = sb("pT", [P, NQ, KT, CQ])
        p_hi = sb("p_hi", [P, RING, PT, CQ], F32R)
        p_lo = sb("p_lo", [P, RING, PT, CQ], F32R)
        rden_bc = sb("rden_bc", [P, N])
        normed = sb("normed", [P, 2, BANK])

        S = psum("S", [P, 2, N])
        ACC = psum("ACC", [P, NQ, CQ])
        BC = psum("BC", [P, BANK])
        VT_PS = psum("VT_PS", [P, BANK])
        w_psum = [S[:, n // 2, BANK * (n % 2):BANK * (n % 2) + P] for n in range(4)]

        x0_loaded, xs_loaded, w_loaded, rows_loaded = map(sem, ("x0_loaded", "xs_loaded", "w_loaded", "rows_loaded"))
        ident_ready, gm_ready, half_ready = map(sem, ("ident_ready", "gm_ready", "half_ready"))
        cols_psum, cols_ready, qbs_ready = map(sem, ("cols_psum", "cols_ready", "qbs_ready"))
        wT_psum, wqk_hi_ready, wqk_lo_ready = map(sem, ("wT_psum", "wqk_hi_ready", "wqk_lo_ready"))
        pwT_ready, wpv_psum, wpv_ready = map(sem, ("pwT_ready", "wpv_psum", "wpv_ready"))
        bias_psum, bias_ready = map(sem, ("bias_psum", "bias_ready"))
        bn_ready, chan_ready, gmean_psum, gmean_ready = map(sem, ("bn_ready", "chan_ready", "gmean_psum", "gmean_ready"))
        dmean_ready, cvar_ready, gvar_psum, gvar_ready = map(sem, ("dmean_ready", "cvar_ready", "gvar_psum", "gvar_ready"))
        rstd_ready, gscale_ready, gms_ready, gshift_ready = map(sem, ("rstd_ready", "gscale_ready", "gms_ready", "gshift_ready"))
        h_ready, h_hi_ready, h_lo_ready, resid_ready = map(sem, ("h_ready", "h_hi_ready", "h_lo_ready", "resid_ready"))
        k_psum, k_hi_ready, k_lo_ready = map(sem, ("k_psum", "k_hi_ready", "k_lo_ready"))
        q_psum, q_hi_ready, q_lo_ready = map(sem, ("q_psum", "q_hi_ready", "q_lo_ready"))
        v_psum, v_hi_ready, v_lo_ready = map(sem, ("v_psum", "v_hi_ready", "v_lo_ready"))
        scores_psum, negmax_ready, probs_ready, blocks_ready = map(sem, ("scores_psum", "negmax_ready", "probs_ready", "blocks_ready"))
        moved = [sem(f"moved{a}") for a in range(NQ)]
        MOVED = 16 * NQ
        p_hi_ready, p_lo_ready, part_done = map(sem, ("p_hi_ready", "p_lo_ready", "part_done"))
        rden_ready, bc_psum, bc_ready = map(sem, ("rden_ready", "bc_psum", "bc_ready"))
        normed_ready, out_ready, stored = map(sem, ("normed_ready", "out_ready", "stored"))

        block = ctx.enter_context(nc.Block())

        @block.sync
        def _(sp):
            sp.dma_start(x_sb[:, 0, :], x[0]).then_inc(x0_loaded, 16)
            for n, v in enumerate((gn_w, gn_b, qb, kb, vb, pb)):
                sp.dma_start(rows[n:n + 1, :], v.rearrange("(a c) -> a c", a=1)).then_inc(rows_loaded, 16)
            for n, w in enumerate((qw, kw, vw, pw)):
                sp.dma_start(w_nat[:, n, :], w).then_inc(w_loaded, 16)
            sp.dma_start(x_sb[:, 1:B, :], x[1:B].rearrange("b c n -> c b n")).then_inc(xs_loaded, 16)

            for b in range(B + 1):
                if b < B:
                    sp.wait_ge(blocks_ready, CH * (b + 1))
                    for a in range(NQ):
                        if b > 0:
                            sp.wait_ge(p_hi_ready, CH * (b - 1) + 2 * (a + 1))
                            sp.wait_ge(p_lo_ready, CH * (b - 1) + 2 * (a + 1))
                        for j in range(NQ):
                            sp.dma_start(pT[Q * j:Q * (j + 1), a].rearrange("p t n -> p (t n)"),
                                         blocks[Q * a:Q * (a + 1), b % 2, j].rearrange("p t c q -> p (t c q)"))\
                              .then_inc(moved[a], 16)
                if b > 0:
                    sp.wait_ge(out_ready, 2 * b)
                    sp.dma_start(out[b - 1], x_sb[:, b - 1, :]).then_inc(stored, 16)
            sp.wait_ge(stored, 16 * B)

        @block.tensor
        def _(pe):
            def group_means(b):
                pe.wait_ge(chan_ready, b + 1)
                pe.matmul(BC[:, 0:1], group_mean[:, :], chan[:, 0:1], start=True, stop=True).then_inc(gmean_psum, 1)

            def group_vars(b):
                pe.wait_ge(cvar_ready, b + 1)
                pe.matmul(BC[:, 2:3], group_mean[:, :], cvar[:, :], start=True, stop=True).then_inc(gvar_psum, 1)

            def project_k(b):
                if b > 0:
                    pe.wait_ge(probs_ready, CH * b - 1)
                pe.wait_ge(h_hi_ready, b + 1)
                for f in range(HALVES):
                    cs = slice(BANK * f, BANK * (f + 1))
                    pe.matmul(S[:, 0, cs], wqk_hi[:, 1, :], h_hi[:, cs], start=True, stop=False)
                    pe.matmul(S[:, 0, cs], wqk_lo[:, 1, :], h_hi[:, cs], start=False, stop=False)
                pe.wait_ge(h_lo_ready, b + 1)
                for f in range(HALVES):
                    cs = slice(BANK * f, BANK * (f + 1))
                    last = pe.matmul(S[:, 0, cs], wqk_hi[:, 1, :], h_lo[:, cs], start=False, stop=True)
                last.then_inc(k_psum, 1)

            def project_q(b):
                if b > 0:
                    pe.wait_ge(probs_ready, CH * b)
                for f in range(HALVES):
                    cs = slice(BANK * f, BANK * (f + 1))
                    pe.matmul(S[:, 1, cs], wqk_lo[:, 0, :], h_hi[:, cs], start=True, stop=False)
                    pe.matmul(S[:, 1, cs], wqk_hi[:, 0, :], h_hi[:, cs], start=False, stop=False)
                    pe.matmul(S[:, 1, cs], wqk_hi[:, 0, :], h_lo[:, cs], start=False, stop=True).then_inc(q_psum, 1)

            def scores(c):
                b, i = c // CH, c % CH
                if i == 0:
                    pe.wait_ge(k_hi_ready, b + 1)
                    pe.wait_ge(k_lo_ready, b + 1)
                    pe.wait_ge(q_hi_ready, 2 * b + 1)
                    pe.wait_ge(q_lo_ready, 2 * b + 1)
                if i == 1:
                    pe.wait_ge(q_hi_ready, 2 * (b + 1))
                    pe.wait_ge(q_lo_ready, 2 * (b + 1))
                if c >= 2:
                    pe.wait_ge(probs_ready, c - 1)
                qs = slice(P * i, P * (i + 1))
                for f in range(HALVES):
                    ks = slice(BANK * f, BANK * (f + 1))
                    pe.matmul(S[:, c % 2, ks], qk_hi[:, 0, qs], qk_hi[:, 1, ks], start=True, stop=False)
                    pe.matmul(S[:, c % 2, ks], qk_hi[:, 0, qs], qk_lo[:, 1, ks], start=False, stop=False)
                for f in range(HALVES):
                    ks = slice(BANK * f, BANK * (f + 1))
                    last = pe.matmul(S[:, c % 2, ks], qk_lo[:, 0, qs], qk_hi[:, 1, ks], start=False, stop=True)
                last.then_inc(scores_psum, 1)

            def value_part(m):
                b, n = m // CH, m % CH
                a, half = n // 2, n % 2
                if n == 0:
                    pe.wait_ge(v_hi_ready, VP * (b + 1))
                    pe.wait_ge(v_lo_ready, VP * (b + 1))
                if n % 4 == 0 and b > 0:
                    pe.wait_ge(normed_ready, 2 * (b - 1) + n // 4 + 1)
                pe.wait_ge(p_hi_ready, m + 1)
                pe.wait_ge(p_lo_ready, m + 1)
                for u in range(PT):
                    t = PT * half + u
                    pe.matmul(ACC[:, a, :], v_hi[:, b % 2, t, :], p_hi[:, m % RING, u, :], start=(t == 0), stop=False)
                    pe.matmul(ACC[:, a, :], v_hi[:, b % 2, t, :], p_lo[:, m % RING, u, :], start=False, stop=False)
                    last = pe.matmul(ACC[:, a, :], v_lo[:, b % 2, t, :], p_hi[:, m % RING, u, :],
                                     start=False, stop=(t == KT - 1))
                last.then_inc(part_done, 1)

            def broadcast_rden(k):
                b, g = k // 2, k % 2
                pe.wait_ge(rden_ready, k + 1)
                if k > 0:
                    pe.wait_ge(bc_ready, k)
                pe.wait_ge(gvar_ready, min(b + 3, B))
                for c in range(GC):
                    col = rden[:, b % 2, GC * g + c:GC * g + c + 1]
                    last = pe.transpose(BC[:, P * c:P * (c + 1)], col.to_broadcast([P, P]), ident[:, :])
                last.then_inc(bc_psum, 1)

            def value_tiles(b, p):
                if b + p > 0:
                    pe.wait_ge(v_hi_ready, VP * b + p)
                    pe.wait_ge(v_lo_ready, VP * b + p)
                for u in range(VT):
                    t = VT * p + u
                    last = pe.matmul(VT_PS[:, P * u:P * (u + 1)], h[:, b % 2, P * t:P * (t + 1)], wpv[:, :],
                                     start=True, stop=True)
                last.then_inc(v_psum, 1)

            pe.wait_ge(ident_ready, 1)
            pe.wait_ge(rows_loaded, 16 * 6)
            pe.transpose(VT_PS[:, 0:6], rows[:, :], ident[0:6, 0:6]).then_inc(cols_psum, 1)
            pe.wait_ge(w_loaded, 16 * 4)
            for n, w in enumerate((0, 1, 3)):
                pe.transpose(w_psum[n], w_nat[:, w, :], ident[:, :]).then_inc(wT_psum, 1)
            pe.wait_ge(gm_ready, 3)
            group_means(0)
            group_vars(0)
            pe.wait_ge(pwT_ready, 1)
            pe.matmul(w_psum[3], w_nat[:, 2, :], pwT[:, :], start=True, stop=True).then_inc(wpv_psum, 1)
            pe.wait_ge(cols_ready, 1)
            pe.wait_ge(gvar_ready, 1)
            pe.matmul(BC[:, 0:1], pwT[:, :], cols[:, VB:VB + 1], start=True, stop=True).then_inc(bias_psum, 1)
            pe.wait_ge(wqk_hi_ready, 2)
            pe.wait_ge(wqk_lo_ready, 2)
            pe.wait_ge(wpv_ready, 1)
            project_k(0)
            project_q(0)

            for c in range(STEPS + LAG):
                b, i = c // CH, c % CH
                if 0 < b < B and i == 0:
                    project_q(b)
                if i == 0 and c >= LAG:
                    value_part(c - LAG)
                if c < STEPS:
                    scores(c)
                if b < B - 1 and i == CH - 1:
                    project_k(b + 1)
                if i != 0 and c >= LAG:
                    value_part(c - LAG)
                if c >= CH and i in (LAG - CH + 1, LAG - CH + 2):
                    broadcast_rden(2 * (b - 1) + i - (LAG - CH + 1))
                if b < B - 1 and i == 1:
                    if b == 0:
                        pe.wait_ge(bias_ready, 1)
                    else:
                        pe.wait_ge(bc_ready, 2 * (b - 1))
                    group_means(b + 1)
                if b < B - 1 and i == 3:
                    group_vars(b + 1)
                if b < B and 0 <= i - V_STEP < VP:
                    value_tiles(b, i - V_STEP)

        @block.scalar
        def _(act):
            def split_h(b):
                act.wait_ge(h_ready, b + 1)
                if b > 0:
                    act.wait_ge(q_psum, 2 * b)
                act.copy(h_hi[:, :], h[:, b % 2, :]).then_inc(h_hi_ready, 1)

            def add_k_bias(b):
                act.wait_ge(k_psum, b + 1)
                if b > 0:
                    act.wait_ge(scores_psum, CH * b)
                act.activation(qk_hi[:, 1, :], S[:, 0, :], ACT.Identity, bias=cols[:, KB:KB + 1]).then_inc(k_hi_ready, 1)

            def add_q_bias(b):
                for f in range(HALVES):
                    act.wait_ge(q_psum, 2 * b + f + 1)
                    cs = slice(BANK * f, BANK * (f + 1))
                    act.activation(qk_hi[:, 0, cs], S[:, 1, cs], ACT.Identity, bias=qb_scaled[:, :]).then_inc(q_hi_ready, 1)

            def exponentials(c):
                i = c % CH
                act.wait_ge(negmax_ready, c + 1)
                if c >= 2:
                    act.wait_ge(blocks_ready, c - 1)
                if c >= CH and i % GC == 0:
                    act.wait_ge(rden_ready, 2 * (c // CH - 1) + i // GC + 1)
                act.activation(probs[:, c % 2, :], S[:, c % 2, :], ACT.Exp, bias=negmax[:, i:i + 1],
                               accum_out=den[:, i:i + 1]).then_inc(probs_ready, 1)

            def split_probs(m):
                b, n = m // CH, m % CH
                a, half = n // 2, n % 2
                if half == 0:
                    act.wait_ge(moved[a], MOVED * (b + 1))
                if m >= RING:
                    act.wait_ge(part_done, m - RING + 1)
                    act.wait_ge(p_lo_ready, m - RING + 1)
                act.copy(p_hi[:, m % RING], pT[:, a, PT * half:PT * (half + 1), :]).then_inc(p_hi_ready, 1)

            def split_v(b, p):
                act.wait_ge(v_psum, VP * b + p + 1)
                if b > 1:
                    act.wait_ge(part_done, CH * (b - 1) - 1 + p // 2)
                act.copy(v_hi[:, b % 2, VT * p:VT * (p + 1), :],
                         VT_PS[:, 0:VT * P].rearrange("p (t c) -> p t c", t=VT)).then_inc(v_hi_ready, 1)

            act.wait_ge(half_ready, 1)
            act.activation(warm[:, :], minus_half[:, :], ACT.Exp)
            act.wait_ge(wT_psum, 1)
            act.mul(wqk_hi[:, 0, :], w_psum[0], SCALE).then_inc(wqk_hi_ready, 1)
            act.wait_ge(wT_psum, 2)
            act.copy(wqk_hi[:, 1, :], w_psum[1]).then_inc(wqk_hi_ready, 1)
            act.wait_ge(wT_psum, 3)
            act.copy(pwT[:, :], w_psum[2]).then_inc(pwT_ready, 1)
            split_h(0)
            act.wait_ge(qbs_ready, 1)
            add_k_bias(0)
            add_q_bias(0)

            for c in range(STEPS + LAG):
                b, i = c // CH, c % CH
                if 0 < b < B and i == 0:
                    add_k_bias(b)
                    add_q_bias(b)
                if 0 <= c + AHEAD - LAG < STEPS:
                    split_probs(c + AHEAD - LAG)
                if c < STEPS:
                    exponentials(c)
                if b < B and i == 1:
                    act.wait_ge(bias_ready, 1)
                    act.wait_ge(h_ready, b + 1)
                    act.activation(x_sb[:, b, :], x_sb[:, b, :], ACT.Identity, bias=out_bias[:, :])\
                       .then_inc(resid_ready, 1)
                if b < B and 0 <= i - V_STEP < VP:
                    split_v(b, i - V_STEP)
                if c >= CH and i in (LAG - CH + 1, LAG - CH + 2):
                    g = i - (LAG - CH + 1)
                    act.wait_ge(bc_psum, 2 * (b - 1) + g + 1)
                    if b > 1:
                        act.wait_ge(normed_ready, 2 * (b - 1))
                    act.copy(rden_bc[:, BANK * g:BANK * (g + 1)], BC[:, :]).then_inc(bc_ready, 1)
                if b < B - 1 and i == CH - 2:
                    split_h(b + 1)

        @block.vector
        def _(dve):
            def channel_stats(b):
                for f in range(HALVES):
                    dve.bn_stats(bn[:, f, :], x_sb[:, b, BANK * f:BANK * (f + 1)]).then_inc(bn_ready, 1)
                dve.wait_ge(bn_ready, HALVES * (b + 1))
                if b > 0:
                    dve.wait_ge(gmean_psum, b)
                    dve.wait_ge(cvar_ready, b)
                dve.bn_aggr(chan[:, :], bn[:, :, :].rearrange("p a b -> p (a b)")).then_inc(chan_ready, 1)

            def channel_vars(b):
                dve.wait_ge(gmean_psum, b + 1)
                if b > 0:
                    dve.wait_ge(gms_ready, b)
                dve.tensor_copy(gmean[:, :], BC[:, 0:1]).then_inc(gmean_ready, 1)
                dve.wait_ge(gmean_ready, b + 1)
                dve.tensor_tensor(dmean[:, :], chan[:, 0:1], gmean[:, :], ALU.subtract).then_inc(dmean_ready, 1)
                dve.wait_ge(dmean_ready, b + 1)
                dve.scalar_tensor_tensor(cvar[:, :], dmean[:, :], dmean[:, 0:1], chan[:, 1:2], ALU.mult, ALU.add)\
                   .then_inc(cvar_ready, 1)

            def group_var(b):
                dve.wait_ge(gvar_psum, b + 1)
                dve.tensor_scalar(gvar[:, :], BC[:, 2:3], EPS, None, ALU.add).then_inc(gvar_ready, 1)

            def shift(b):
                dve.wait_ge(gscale_ready, b + 1)
                dve.tensor_tensor(gms[:, :], gmean[:, :], gscale[:, :], ALU.mult).then_inc(gms_ready, 1)
                dve.wait_ge(gms_ready, b + 1)
                dve.tensor_tensor(gshift[:, :], cols[:, GNB:GNB + 1], gms[:, :], ALU.subtract).then_inc(gshift_ready, 1)

            def normalize(b):
                dve.wait_ge(gshift_ready, b + 1)
                if b > 0:
                    dve.wait_ge(v_psum, VP * b)
                dve.tensor_scalar(h[:, b % 2, :], x_sb[:, b, :], gscale[:, :], gshift[:, :], ALU.mult, ALU.add)\
                   .then_inc(h_ready, 1)

            def split_k(b):
                dve.wait_ge(k_hi_ready, b + 1)
                dve.scalar_tensor_tensor(qk_lo[:, 1, :], S[:, 0, :], cols[:, KB:KB + 1], qk_hi[:, 1, :].bitcast(F32),
                                         ALU.add, ALU.subtract).then_inc(k_lo_ready, 1)

            def split_q(b):
                for f in range(HALVES):
                    dve.wait_ge(q_hi_ready, 2 * b + f + 1)
                    cs = slice(BANK * f, BANK * (f + 1))
                    dve.scalar_tensor_tensor(qk_lo[:, 0, cs], S[:, 1, cs], qb_scaled[:, :], qk_hi[:, 0, cs].bitcast(F32),
                                             ALU.add, ALU.subtract).then_inc(q_lo_ready, 1)

            def row_max(c):
                i = c % CH
                dve.wait_ge(scores_psum, c + 1)
                dve.tensor_reduce(negmax[:, i:i + 1], S[:, c % 2, :], AX.X, ALU.max, negate=True)\
                   .then_inc(negmax_ready, 1)

            def transpose_blocks(c):
                b, i = c // CH, c % CH
                dve.wait_ge(probs_ready, c + 1)
                if i == 0 and b > 1:
                    for a in range(NQ):
                        dve.wait_ge(moved[a], MOVED * (b - 1))
                dve.transpose(blocks[:, b % 2, :, :, i, :].rearrange("p j t q -> p t j q"),
                              probs[:, c % 2, :].rearrange("p (t j q) -> p t j q", t=KT, j=NQ)).then_inc(blocks_ready, 1)
                if i % GC == GC - 1:
                    g = i // GC
                    if b > 1:
                        dve.wait_ge(bc_psum, 2 * (b - 2) + g + 1)
                    dve.reciprocal(rden[:, b % 2, GC * g:GC * (g + 1)], den[:, GC * g:GC * (g + 1)])\
                       .then_inc(rden_ready, 1)

            def divide(b, half):
                dve.wait_ge(part_done, CH * b + 4 * (half + 1))
                dve.wait_ge(bc_ready, 2 * (b + 1))
                if b > 0:
                    dve.wait_ge(out_ready, 2 * (b - 1) + half + 1)
                a = slice(2 * half, 2 * half + 2)
                dve.tensor_tensor(normed[:, half, :].rearrange("p (c a q) -> p c a q", c=CH, a=2),
                                  ACC[:, a, :].rearrange("p a (c q) -> p c a q", c=CH),
                                  rden_bc[:, :].rearrange("p (c a q) -> p c a q", c=CH, a=NQ)[:, :, a, :], ALU.mult)\
                   .then_inc(normed_ready, 1)

            def split_v(b, p):
                dve.wait_ge(v_hi_ready, VP * b + p + 1)
                ts = slice(VT * p, VT * (p + 1))
                dve.tensor_tensor(v_lo[:, b % 2, ts, :], VT_PS[:, 0:VT * P].rearrange("p (t c) -> p t c", t=VT),
                                  v_hi[:, b % 2, ts, :].bitcast(F32), ALU.subtract).then_inc(v_lo_ready, 1)

            dve.memset(minus_half[:, :], -0.5).then_inc(half_ready, 1)
            dve.wait_ge(x0_loaded, 16)
            channel_stats(0)
            dve.wait_ge(cols_psum, 1)
            dve.tensor_copy(cols[:, :], VT_PS[:, 0:6]).then_inc(cols_ready, 1)
            dve.wait_ge(cols_ready, 1)
            dve.tensor_scalar(qb_scaled[:, :], cols[:, QB:QB + 1], SCALE, None, ALU.mult).then_inc(qbs_ready, 1)
            channel_vars(0)
            group_var(0)
            for w, scale in ((0, SCALE), (1, 1.0)):
                dve.wait_ge(wqk_hi_ready, w + 1)
                dve.scalar_tensor_tensor(wqk_lo[:, w, :], w_psum[w], scale, wqk_hi[:, w, :].bitcast(F32),
                                         ALU.mult, ALU.subtract).then_inc(wqk_lo_ready, 1)
            shift(0)
            normalize(0)
            dve.wait_ge(wpv_psum, 1)
            dve.tensor_copy(wpv[:, :], w_psum[3]).then_inc(wpv_ready, 1)
            dve.wait_ge(bias_psum, 1)
            dve.tensor_tensor(out_bias[:, :], BC[:, 0:1], cols[:, PB:PB + 1], ALU.add).then_inc(bias_ready, 1)
            split_k(0)
            split_q(0)
            dve.wait_ge(xs_loaded, 16)

            for c in range(STEPS + LAG + 1):
                b, i = c // CH, c % CH
                if c > 0 and i == 0 and b <= B:
                    transpose_blocks(c - 1)
                if 0 < b < B and i == 0:
                    split_k(b)
                    split_q(b)
                if c < STEPS:
                    row_max(c)
                if i > 0 and c < STEPS:
                    transpose_blocks(c - 1)
                if c >= LAG + 4 and (c - LAG) % 4 == 0:
                    m = c - LAG - 4
                    divide(m // CH, m % CH // 4)
                if b < B - 1 and i == 0:
                    channel_stats(b + 1)
                if b < B - 1 and i == 2:
                    channel_vars(b + 1)
                if b < B - 1 and i == 4:
                    group_var(b + 1)
                if b < B and 0 <= i - V_STEP < VP:
                    split_v(b, i - V_STEP)
                if b < B - 1 and i == 5:
                    shift(b + 1)
                    normalize(b + 1)

        @block.gpsimd
        def _(pool):
            def group_scale(b):
                pool.wait_ge(gvar_ready, b + 1)
                if b > 0:
                    pool.wait_ge(h_ready, b)
                pool.tensor_tensor(rstd[:, :], gvar[:, :], minus_half[:, :], ALU.pow).then_inc(rstd_ready, 1)
                pool.wait_ge(rstd_ready, b + 1)
                pool.tensor_tensor(gscale[:, :], rstd[:, :], cols[:, GNW:GNW + 1], ALU.mult).then_inc(gscale_ready, 1)

            def split_h(b):
                pool.wait_ge(h_hi_ready, b + 1)
                pool.tensor_tensor(h_lo[:, :], h[:, b % 2, :], h_hi[:, :].bitcast(F32), ALU.subtract).then_inc(h_lo_ready, 1)

            def split_probs(m):
                n = m % CH
                a, half = n // 2, n % 2
                pool.wait_ge(p_hi_ready, m + 1)
                pool.tensor_tensor(p_lo[:, m % RING], pT[:, a, PT * half:PT * (half + 1), :],
                                   p_hi[:, m % RING].bitcast(F32), ALU.subtract).then_inc(p_lo_ready, 1)

            def add_residual(b, half):
                pool.wait_ge(normed_ready, 2 * b + half + 1)
                pool.wait_ge(resid_ready, b + 1)
                xs = x_sb[:, b, :].rearrange("p (c h r) -> p c h r", c=CH, h=2)[:, :, half, :]
                pool.tensor_tensor(xs, normed[:, half, :].rearrange("p (c r) -> p c r", c=CH), xs, ALU.add)\
                    .then_inc(out_ready, 1)

            pool.memset(ident[:, :], 0.0).then_inc(gm_ready, 1)
            pool.wait_ge(gm_ready, 1)
            pool.affine_select(out=ident[:, :], in_=ident[:, :], compare_op=ALU.not_equal, fill=1.0, base=0,
                               pattern=[[-1, P]], channel_multiplier=1).then_inc(ident_ready, 1)
            gm = group_mean[:, :].rearrange("p (g c) -> p g c", g=GROUPS)
            pool.memset(group_mean[:, :], 1.0 / CPG).then_inc(gm_ready, 1)
            pool.wait_ge(gm_ready, 2)
            pool.affine_select(out=gm, in_=gm, compare_op=ALU.is_ge, fill=0.0, base=0,
                               pattern=[[-CPG, GROUPS], [0, CPG]], channel_multiplier=1).then_inc(ident_ready, 1)
            pool.wait_ge(ident_ready, 2)
            pool.affine_select(out=gm, in_=gm, compare_op=ALU.is_ge, fill=0.0, base=CPG - 1,
                               pattern=[[CPG, GROUPS], [0, CPG]], channel_multiplier=-1).then_inc(gm_ready, 1)
            pool.wait_ge(half_ready, 1)
            pool.wait_ge(cols_ready, 1)
            group_scale(0)
            split_h(0)

            for c in range(STEPS + LAG + 1):
                b, i = c // CH, c % CH
                if 0 <= c + AHEAD - LAG < STEPS:
                    split_probs(c + AHEAD - LAG)
                if b < B - 1 and i == 4:
                    group_scale(b + 1)
                if b < B - 1 and i == CH - 2:
                    split_h(b + 1)
                if c >= LAG + 4 and (c - LAG) % 4 == 0:
                    m = c - LAG - 4
                    add_residual(m // CH, m % CH // 4)


def kernel(x, L0_conv_gn_w, L0_conv_gn_b, L0_conv_qw, L0_conv_qb, L0_conv_kw, L0_conv_kb,
           L0_conv_vw, L0_conv_vb, L0_conv_pw, L0_conv_pb):
    import numpy as np
    import concourse.bacc as bacc
    from concourse.bass_utils import run_bass_kernel_spmd

    B, C, H, W = x.shape
    given = {
        "x": np.asarray(x).reshape(B, C, H * W),
        "gn_w": L0_conv_gn_w, "gn_b": L0_conv_gn_b, "qw": L0_conv_qw, "qb": L0_conv_qb,
        "kw": L0_conv_kw, "kb": L0_conv_kb, "vw": L0_conv_vw, "vb": L0_conv_vb,
        "pw": L0_conv_pw, "pb": L0_conv_pb,
    }
    arrays = {name: np.ascontiguousarray(a) for name, a in given.items()}
    nc = bacc.Bacc("TRN2", target_bir_lowering=False, num_devices=1)
    ins = {n: nc.dram_tensor(n, a.shape, mybir.dt.from_np(a.dtype), kind="ExternalInput").ap()
           for n, a in arrays.items()}
    out = nc.dram_tensor("out", arrays["x"].shape, F32, kind="ExternalOutput").ap()
    build(nc, **ins, out=out)
    got = run_bass_kernel_spmd(nc, [arrays], core_ids=[0])
    return got.results[0]["out"].reshape(B, C, H, W)
```

```python
from contextlib import ExitStack

import concourse.bass as bass
from concourse import mybir
from concourse.alu_op_type import AluOpType as ALU

F32 = mybir.dt.float32
F32R = mybir.dt.float32r
ACT = mybir.ActivationFunctionType
AX = mybir.AxisListType

P = 128
Q = 32
NQ = P // Q
GROUPS = 8
EPS = 1e-5
BANK = 512
LAG = 12
AHEAD = 3
RING = 4
TAIL_SPLIT = (1, 1, 1, 2, 2, 1)
TAIL_MULTIPLIED = (1, 1, 2, 2, 2)


def build(nc, x, vectors, weights, out):
    B, C, N = x.shape
    CH = N // P
    KT = CH
    CQ = CH * Q
    HALVES = N // BANK
    PT = KT // 2
    GC = BANK // P
    VP = 2
    VT = KT // VP
    SCALE = float(C) ** -0.5
    CPG = C // GROUPS
    STEPS = B * CH
    L = B - 1
    PAIRS = CH // 2
    PN = 2 * P
    DIRECT = CH * L
    assert B > 2 and B % 2 == 0 and C == P and HALVES == 2 and 2 * NQ == CH and 2 * CQ == BANK and CQ * PT == N

    with ExitStack() as ctx:
        def sb(name, shape, dt=F32):
            return ctx.enter_context(nc.sbuf_tensor(name, shape, dt))

        def psum(name, shape):
            return ctx.enter_context(nc.psum_tensor(name, shape, F32))

        def sem(name):
            return ctx.enter_context(nc.semaphore(name))

        x_sb = sb("x_sb", [P, B, N])
        w_in = sb("w_in", [P, 4, P])
        QW, KW, PW, VW = range(4)
        cols = sb("cols", [P, 6])
        GNW, GNB, QB, KB, VB, PB = range(6)
        qb_scaled = sb("qb_scaled", [P, 1])
        out_bias = sb("out_bias", [P, 1])
        ident = sb("ident", [P, P])
        group_mean = sb("group_mean", [P, P])
        minus_half = sb("minus_half", [P, 1])
        warm = sb("warm", [P, 1])
        wqk_hi = sb("wqk_hi", [P, 2, P], F32R)
        wqk_lo = sb("wqk_lo", [P, 2, P], F32R)
        wpv = sb("wpv", [P, P])
        bn = sb("bn", [P, HALVES, 6])
        chan = sb("chan", [P, 2])
        gmean = sb("gmean", [P, 1])
        dmean = sb("dmean", [P, 1])
        cvar = sb("cvar", [P, 1])
        gvar = sb("gvar", [P, 1])
        rstd = sb("rstd", [P, 1])
        gscale = sb("gscale", [P, 1])
        gms = sb("gms", [P, 1])
        gshift = sb("gshift", [P, 1])
        h = sb("h", [P, N])
        h_hi = sb("h_hi", [P, N], F32R)
        h_lo = sb("h_lo", [P, N], F32R)
        qk_hi = sb("qk_hi", [P, 2, N], F32R)
        qk_lo = sb("qk_lo", [P, 2, N], F32R)
        v_hi = sb("v_hi", [P, 2, KT, P], F32R)
        v_lo = sb("v_lo", [P, 2, KT, P], F32R)
        negmax = sb("negmax", [P, CH])
        den = sb("den", [P, CH])
        rden = sb("rden", [P, 2, CH])
        probs = sb("probs", [P, 2, N])
        pT = sb("pT", [P, NQ, KT, CQ])
        p_hi = sb("p_hi", [P, RING, PT, CQ], F32R)
        p_lo = sb("p_lo", [P, RING, PT, CQ], F32R)
        rden_bc = sb("rden_bc", [P, N])
        vL_hi, vL_lo = (v[:, :].rearrange("p (t c) -> p t c", t=KT) for v in (h_hi, h_lo))
        rdenL_bc = h[:, :]

        blocks = [sb("blocks0", [P, NQ, KT, CH, Q]), None]
        with nc.sbuf_tensor("blocks1", [P, NQ, KT, CH, Q], F32) as blocks1:
            blocks[1] = blocks1
        pair_hi = sb("pair_hi", [P, 2, KT, 2, P], F32R)
        pair_lo = sb("pair_lo", [P, 2, KT, 2, P], F32R)

        S = psum("S", [P, 2, N])
        ACC = psum("ACC", [P, NQ, CQ])
        BC = psum("BC", [P, BANK])
        VT_PS = psum("VT_PS", [P, BANK])
        pair_out = [VT_PS[:, 0:PN], VT_PS[:, PN:2 * PN], VT_PS[:, 0:PN], ACC[:, 0, :]]

        x0_loaded = [sem(f"x0_loaded{f}") for f in range(HALVES)]
        xs_loaded, w_loaded, cols_loaded = map(sem, ("xs_loaded", "w_loaded", "cols_loaded"))
        ident_ready, gm_ready, half_ready = map(sem, ("ident_ready", "gm_ready", "half_ready"))
        qbs_ready, wqk_hi_ready, wqk_lo_ready = map(sem, ("qbs_ready", "wqk_hi_ready", "wqk_lo_ready"))
        pv_psum, wpv_ready, bias_ready = map(sem, ("pv_psum", "wpv_ready", "bias_ready"))
        bn_ready, chan_ready, gmean_psum, gmean_ready = map(sem, ("bn_ready", "chan_ready", "gmean_psum", "gmean_ready"))
        dmean_ready, cvar_ready, gvar_psum, gvar_ready = map(sem, ("dmean_ready", "cvar_ready", "gvar_psum", "gvar_ready"))
        rstd_ready, gscale_ready, gms_ready, gshift_ready = map(sem, ("rstd_ready", "gscale_ready", "gms_ready", "gshift_ready"))
        h_ready, h_hi_ready, h_lo_ready = map(sem, ("h_ready", "h_hi_ready", "h_lo_ready"))
        resid_ready = sem("resid_ready")
        k_psum, k_hi_ready, k_lo_ready = map(sem, ("k_psum", "k_hi_ready", "k_lo_ready"))
        q_psum, q_hi_ready, q_lo_ready = map(sem, ("q_psum", "q_hi_ready", "q_lo_ready"))
        v_psum, v_hi_ready, v_lo_ready = map(sem, ("v_psum", "v_hi_ready", "v_lo_ready"))
        scores_psum, negmax_ready, probs_ready, blocks_ready = map(sem, ("scores_psum", "negmax_ready", "probs_ready", "blocks_ready"))
        moved = [sem(f"moved{a}") for a in range(NQ)]
        MOVED = 16 * NQ
        p_hi_ready, p_lo_ready, part_done = map(sem, ("p_hi_ready", "p_lo_ready", "part_done"))
        rden_ready, bc_psum, bc_ready = map(sem, ("rden_ready", "bc_psum", "bc_ready"))
        pT_psum, pair_hi_ready, pair_lo_ready, pair_done = map(sem, ("pT_psum", "pair_hi_ready", "pair_lo_ready", "pair_done"))
        pair_normed, pair_out_ready = map(sem, ("pair_normed", "pair_out_ready"))
        normed_ready, out_ready, stored = map(sem, ("normed_ready", "out_ready", "stored"))

        def parts_of(c, lag, tail):
            t = c - CH * (L - 1) - lag
            if t < 0:
                return range(max(c - lag, 0), max(c - lag + 1, 0))
            first = CH * (L - 1) + sum(tail[:t])
            return range(first, first + sum(tail[t:t + 1]))

        def parts_split(c):
            return parts_of(c, LAG - AHEAD, TAIL_SPLIT)

        def parts_multiplied(c):
            return parts_of(c, LAG, TAIL_MULTIPLIED)

        block = ctx.enter_context(nc.Block())

        @block.sync
        def _(sp):
            for f in range(HALVES):
                cs = slice(BANK * f, BANK * (f + 1))
                sp.dma_start(x_sb[:, 0, cs], x[0, :, cs]).then_inc(x0_loaded[f], 16)
            sp.dma_start(cols[:, :], vectors).then_inc(cols_loaded, 16)
            sp.dma_start(w_in[:, :, :], weights.rearrange("n a b -> a n b")).then_inc(w_loaded, 16)
            sp.dma_start(x_sb[:, 1:B, :], x[1:B].rearrange("b c n -> c b n")).then_inc(xs_loaded, 16)

            for b in range(B):
                if b < L:
                    sp.wait_ge(blocks_ready, CH * (b + 1))
                    for a in range(NQ):
                        if b > 0:
                            sp.wait_ge(p_hi_ready, CH * (b - 1) + 2 * (a + 1))
                            sp.wait_ge(p_lo_ready, CH * (b - 1) + 2 * (a + 1))
                        for j in range(NQ):
                            sp.dma_start(pT[Q * j:Q * (j + 1), a].rearrange("p t n -> p (t n)"),
                                         blocks[b % 2][Q * a:Q * (a + 1), j].rearrange("p t c q -> p (t c q)"))\
                              .then_inc(moved[a], 16)
                if 0 < b < L:
                    sp.wait_ge(out_ready, 2 * b)
                    sp.dma_start(out[b - 1], x_sb[:, b - 1, :]).then_inc(stored, 16)
            sp.wait_ge(pair_out_ready, 2)
            sp.dma_start(out[L, :, 0:BANK], x_sb[:, L, 0:BANK]).then_inc(stored, 16)
            sp.wait_ge(out_ready, 2 * L)
            sp.dma_start(out[L - 1], x_sb[:, L - 1, :]).then_inc(stored, 16)
            for r in range(PAIRS // 2, PAIRS):
                sp.wait_ge(pair_out_ready, r + 1)
                cs = slice(PN * r, PN * (r + 1))
                sp.dma_start(out[L, :, cs], x_sb[:, L, cs]).then_inc(stored, 16)
            sp.wait_ge(stored, 16 * (B + PAIRS // 2))

        @block.tensor
        def _(pe):
            def group_means(b):
                pe.wait_ge(chan_ready, b + 1)
                pe.matmul(BC[:, 0:1], group_mean[:, :], chan[:, 0:1], start=True, stop=True).then_inc(gmean_psum, 1)

            def group_vars(b):
                pe.wait_ge(cvar_ready, b + 1)
                pe.matmul(BC[:, 2:3], group_mean[:, :], cvar[:, :], start=True, stop=True).then_inc(gvar_psum, 1)

            def project_k(b):
                if b > 0:
                    pe.wait_ge(probs_ready, CH * b - 1)
                for f in range(HALVES):
                    pe.wait_ge(h_hi_ready, HALVES * b + f + 1)
                    cs = slice(BANK * f, BANK * (f + 1))
                    pe.matmul(S[:, 0, cs], wqk_hi[:, 1, :], h_hi[:, cs], start=True, stop=False)
                    pe.matmul(S[:, 0, cs], wqk_lo[:, 1, :], h_hi[:, cs], start=False, stop=False)
                    pe.wait_ge(h_lo_ready, HALVES * b + f + 1)
                    pe.matmul(S[:, 0, cs], wqk_hi[:, 1, :], h_lo[:, cs], start=False, stop=True).then_inc(k_psum, 1)

            def project_q(b):
                if b > 0:
                    pe.wait_ge(probs_ready, CH * b)
                for f in range(HALVES):
                    cs = slice(BANK * f, BANK * (f + 1))
                    pe.matmul(S[:, 1, cs], wqk_lo[:, 0, :], h_hi[:, cs], start=True, stop=False)
                    pe.matmul(S[:, 1, cs], wqk_hi[:, 0, :], h_hi[:, cs], start=False, stop=False)
                    pe.matmul(S[:, 1, cs], wqk_hi[:, 0, :], h_lo[:, cs], start=False, stop=True).then_inc(q_psum, 1)

            def scores(c):
                b, i = c // CH, c % CH
                if i == 0:
                    pe.wait_ge(k_hi_ready, HALVES * (b + 1))
                    pe.wait_ge(k_lo_ready, HALVES * (b + 1))
                    pe.wait_ge(q_hi_ready, 2 * b + 1)
                    pe.wait_ge(q_lo_ready, 2 * b + 1)
                if i == 1:
                    pe.wait_ge(q_hi_ready, 2 * (b + 1))
                    pe.wait_ge(q_lo_ready, 2 * (b + 1))
                if c >= 2:
                    pe.wait_ge(probs_ready, c - 1)
                if c >= DIRECT + 2:
                    pe.wait_ge(pair_hi_ready, 2 * (c - 1 - DIRECT))
                    pe.wait_ge(pair_lo_ready, 2 * (c - 1 - DIRECT))
                qs = slice(P * i, P * (i + 1))
                for f in range(HALVES):
                    ks = slice(BANK * f, BANK * (f + 1))
                    pe.matmul(S[:, c % 2, ks], qk_hi[:, 0, qs], qk_hi[:, 1, ks], start=True, stop=False)
                    pe.matmul(S[:, c % 2, ks], qk_hi[:, 0, qs], qk_lo[:, 1, ks], start=False, stop=False)
                for f in range(HALVES):
                    ks = slice(BANK * f, BANK * (f + 1))
                    last = pe.matmul(S[:, c % 2, ks], qk_lo[:, 0, qs], qk_hi[:, 1, ks], start=False, stop=True)
                last.then_inc(scores_psum, 1)

            def value_part(m):
                b, n = m // CH, m % CH
                a, half = n // 2, n % 2
                if n == 0:
                    pe.wait_ge(v_hi_ready, VP * (b + 1))
                    pe.wait_ge(v_lo_ready, VP * (b + 1))
                if n % 4 == 0 and b > 0:
                    pe.wait_ge(normed_ready, 2 * (b - 1) + n // 4 + 1)
                pe.wait_ge(p_hi_ready, m + 1)
                pe.wait_ge(p_lo_ready, m + 1)
                for u in range(PT):
                    t = PT * half + u
                    pe.matmul(ACC[:, a, :], v_hi[:, b % 2, t, :], p_hi[:, m % RING, u, :], start=(t == 0), stop=False)
                    pe.matmul(ACC[:, a, :], v_hi[:, b % 2, t, :], p_lo[:, m % RING, u, :], start=False, stop=False)
                    last = pe.matmul(ACC[:, a, :], v_lo[:, b % 2, t, :], p_hi[:, m % RING, u, :],
                                     start=False, stop=(t == KT - 1))
                last.then_inc(part_done, 1)

            def broadcast_rden(k):
                b, g = k // 2, k % 2
                pe.wait_ge(rden_ready, k + 1)
                if k > 0:
                    pe.wait_ge(bc_ready, k)
                pe.wait_ge(gvar_ready, min(b + 3, B))
                for c in range(GC):
                    col = rden[:, b % 2, GC * g + c:GC * g + c + 1]
                    last = pe.transpose(BC[:, P * c:P * (c + 1)], col.to_broadcast([P, P]), ident[:, :])
                last.then_inc(bc_psum, 1)

            def transpose_probs(c):
                pe.wait_ge(probs_ready, c + 1)
                for t in range(KT):
                    last = pe.transpose(S[:, c % 2, P * t:P * (t + 1)], probs[:, c % 2, P * t:P * (t + 1)], ident[:, :])
                    if t % (KT // 2) == KT // 2 - 1:
                        last.then_inc(pT_psum, 1)

            def value_pair(r, half):
                if half == 0:
                    pe.wait_ge(v_hi_ready, VP * B)
                    pe.wait_ge(v_lo_ready, VP * B)
                    pe.wait_ge(pair_hi_ready, 4 * (r + 1))
                    pe.wait_ge(pair_lo_ready, 4 * (r + 1))
                    if r == 2:
                        pe.wait_ge(pair_normed, 2)
                    if r == 3:
                        pe.wait_ge(normed_ready, 2 * L - 1)
                for t in range(PT * half, PT * (half + 1)):
                    hi, lo = (p[:, r % 2, t].rearrange("p d q -> p (d q)") for p in (pair_hi, pair_lo))
                    pe.matmul(pair_out[r], vL_hi[:, t, :], hi, start=(t == 0), stop=False)
                    pe.matmul(pair_out[r], vL_hi[:, t, :], lo, start=False, stop=False)
                    last = pe.matmul(pair_out[r], vL_lo[:, t, :], hi, start=False, stop=(t == KT - 1))
                if half == 1:
                    last.then_inc(pair_done, 1)

            def value_tiles(b, p):
                pe.wait_ge(wpv_ready, 1)
                if b + p > 0:
                    pe.wait_ge(v_hi_ready, VP * b + p)
                    pe.wait_ge(v_lo_ready, VP * b + p)
                for u in range(VT):
                    t = VT * p + u
                    last = pe.matmul(VT_PS[:, P * u:P * (u + 1)], h[:, P * t:P * (t + 1)], wpv[:, :],
                                     start=True, stop=True)
                last.then_inc(v_psum, 1)

            pe.wait_ge(gm_ready, 3)
            group_means(0)
            group_vars(0)
            pe.wait_ge(w_loaded, 16)
            pe.wait_ge(gvar_ready, 1)
            pe.matmul(BC[:, 0:P], w_in[:, VW, :], w_in[:, PW, :], start=True, stop=True)
            pe.wait_ge(cols_loaded, 16)
            pe.matmul(BC[:, P:P + 1], w_in[:, PW, :], cols[:, VB:VB + 1], start=True, stop=True).then_inc(pv_psum, 1)
            pe.wait_ge(wqk_hi_ready, 2)
            pe.wait_ge(wqk_lo_ready, 2)
            project_k(0)
            project_q(0)
            pe.wait_ge(ident_ready, 1)

            for c in range(STEPS + 2):
                b, i = c // CH, c % CH
                if i == 0 and b < B:
                    for m in parts_multiplied(c):
                        value_part(m)
                if b < L and i == 4:
                    group_vars(b + 1)
                if b == L and i == 1:
                    value_tiles(b, 0)
                if c < STEPS:
                    scores(c)
                if 0 < b < L and i == 5:
                    broadcast_rden(2 * (b - 1))
                if b == 0 and i == 6 or 0 < b < L and i == 5:
                    value_tiles(b, 1)
                if c == DIRECT + GC + 2:
                    broadcast_rden(2 * L)
                if c == STEPS:
                    broadcast_rden(2 * L + 1)
                if i != 0 or b == B:
                    for m in parts_multiplied(c)[:1]:
                        value_part(m)
                if 0 < b < L and i == 6:
                    broadcast_rden(2 * (b - 1) + 1)
                if b == 0 and i == 4 or 0 < b < L and i == 3:
                    value_tiles(b, 0)
                if c > DIRECT and c <= STEPS:
                    transpose_probs(c - 1)
                for m in parts_multiplied(c)[1:]:
                    value_part(m)
                if c >= DIRECT + 3:
                    value_pair((c - DIRECT - 3) // 2, (c - DIRECT - 3) % 2)
                if b < L and i == CH - 1:
                    project_k(b + 1)
                    project_q(b + 1)
                if b == L and i == 4:
                    broadcast_rden(2 * (b - 1))
                if b == L and i == 5:
                    broadcast_rden(2 * (b - 1) + 1)
                if b < L and i == 2:
                    if b == 0:
                        pe.wait_ge(bias_ready, 1)
                        pe.wait_ge(wpv_ready, 1)
                    if b > 1:
                        pe.wait_ge(bc_ready, 2 * (b - 1))
                    group_means(b + 1)
                if b == L and i == 1:
                    value_tiles(b, 1)
            value_pair(PAIRS - 1, 1)

        @block.scalar
        def _(act):
            def normalize_hi(b, f0, f1):
                act.wait_ge(gshift_ready, b + 1)
                if b > 0:
                    act.wait_ge(q_psum, HALVES * b)
                cs = slice(BANK * f0, BANK * f1)
                act.activation(h_hi[:, cs], x_sb[:, b, cs], ACT.Identity, bias=gshift[:, :], scale=gscale[:, :])\
                   .then_inc(h_hi_ready, f1 - f0)

            def add_k_bias(b):
                if b > 0:
                    act.wait_ge(scores_psum, CH * b)
                for f in range(HALVES):
                    act.wait_ge(k_psum, HALVES * b + f + 1)
                    cs = slice(BANK * f, BANK * (f + 1))
                    act.activation(qk_hi[:, 1, cs], S[:, 0, cs], ACT.Identity, bias=cols[:, KB:KB + 1])\
                       .then_inc(k_hi_ready, 1)

            def add_q_bias(b):
                for f in range(HALVES):
                    act.wait_ge(q_psum, 2 * b + f + 1)
                    cs = slice(BANK * f, BANK * (f + 1))
                    act.activation(qk_hi[:, 0, cs], S[:, 1, cs], ACT.Identity, bias=qb_scaled[:, :]).then_inc(q_hi_ready, 1)

            def exponentials(c):
                i = c % CH
                act.wait_ge(negmax_ready, c + 1)
                if c >= DIRECT + 2:
                    act.wait_ge(pT_psum, 2 * (c - 1 - DIRECT))
                elif c >= 2:
                    act.wait_ge(blocks_ready, c - 1)
                if c >= CH and i % GC == 0:
                    act.wait_ge(rden_ready, 2 * (c // CH - 1) + i // GC + 1)
                act.activation(probs[:, c % 2, :], S[:, c % 2, :], ACT.Exp, bias=negmax[:, i:i + 1],
                               accum_out=den[:, i:i + 1]).then_inc(probs_ready, 1)

            def split_probs(m):
                b, n = m // CH, m % CH
                a, half = n // 2, n % 2
                if half == 0:
                    act.wait_ge(moved[a], MOVED * (b + 1))
                if m >= RING:
                    act.wait_ge(part_done, m - RING + 1)
                    act.wait_ge(p_lo_ready, m - RING + 1)
                act.copy(p_hi[:, m % RING], pT[:, a, PT * half:PT * (half + 1), :]).then_inc(p_hi_ready, 1)

            def split_v(b, p):
                act.wait_ge(v_psum, VP * b + p + 1)
                if b == L:
                    act.copy(vL_hi[:, VT * p:VT * (p + 1), :],
                             VT_PS[:, :].rearrange("p (t c) -> p t c", t=VT)).then_inc(v_hi_ready, 1)
                    return
                if b > 1:
                    act.wait_ge(part_done, CH * (b - 1) - 1 + p)
                act.copy(v_hi[:, b % 2, VT * p:VT * (p + 1), :],
                         VT_PS[:, 0:VT * P].rearrange("p (t c) -> p t c", t=VT)).then_inc(v_hi_ready, 1)

            def split_pairs(c):
                r, d = (c - DIRECT) // 2, c % 2
                for f in range(2):
                    act.wait_ge(pT_psum, 2 * (c - DIRECT) + f + 1)
                    if c == DIRECT and f == 0:
                        for a in range(NQ):
                            act.wait_ge(moved[a], MOVED * (L - 1))
                    if r > 1:
                        act.wait_ge(pair_done, r - 1)
                        act.wait_ge(pair_lo_ready, 4 * (r - 1))
                    ts = slice(PT * f, PT * (f + 1))
                    act.copy(pair_hi[:, r % 2, ts, d, :], S[:, c % 2, BANK * f:BANK * (f + 1)]
                             .rearrange("p (t q) -> p t q", t=PT)).then_inc(pair_hi_ready, 1)

            def copy_rden(b, g):
                act.wait_ge(bc_psum, 2 * b + g + 1)
                if b > 0:
                    act.wait_ge(out_ready, 2 * b)
                act.copy(rden_bc[:, BANK * g:BANK * (g + 1)], BC[:, :]).then_inc(bc_ready, 1)

            def add_bias(b):
                act.wait_ge(bias_ready, 1)
                act.wait_ge(h_ready, HALVES * (b + 1))
                act.wait_ge(h_hi_ready, HALVES * (b + 1))
                act.activation(x_sb[:, b, :], x_sb[:, b, :], ACT.Identity, bias=out_bias[:, :]).then_inc(resid_ready, 1)

            act.wait_ge(half_ready, 1)
            act.activation(warm[:, :], minus_half[:, :], ACT.Exp)
            act.wait_ge(w_loaded, 16)
            act.mul(wqk_hi[:, 0, :], w_in[:, QW, :], SCALE).then_inc(wqk_hi_ready, 1)
            act.copy(wqk_hi[:, 1, :], w_in[:, KW, :]).then_inc(wqk_hi_ready, 1)
            for f in range(HALVES):
                normalize_hi(0, f, f + 1)
            act.wait_ge(qbs_ready, 1)
            add_k_bias(0)
            add_q_bias(0)

            split_first = ((4, 5, 6, 7),) * L + ((0, 1, 2, 4, 5, 6, 7), (0,))
            for c in range(STEPS + 1):
                b, i = c // CH, c % CH
                if 0 < b < B and i == 0:
                    add_k_bias(b)
                    add_q_bias(b)
                if c > DIRECT:
                    split_pairs(c - 1)
                if b == L and i == 5:
                    copy_rden(b - 1, 1)
                if b < L and i == 6:
                    normalize_hi(b + 1, 0, HALVES)
                first = 1 if i in split_first[b] else 0
                for m in parts_split(c)[:first]:
                    split_probs(m)
                if b == 0 and i == 4 or 0 < b < L and i == 3 or b == L and i == 0:
                    split_v(b, 0)
                if b == 0 and i == 6 or 0 < b < L and i == 5:
                    split_v(b, 1)
                if c < STEPS:
                    exponentials(c)
                if b < B and i == 1:
                    add_bias(b)
                for m in parts_split(c)[first:]:
                    split_probs(m)
                if c == DIRECT + GC + 2 or c == STEPS:
                    g = (c - DIRECT) // CH
                    act.wait_ge(bc_psum, 2 * L + g + 1)
                    act.wait_ge(v_psum, VP * B)
                    act.copy(rdenL_bc[:, BANK * g:BANK * (g + 1)], BC[:, :]).then_inc(bc_ready, 1)
                if b == L and i == 1:
                    split_v(b, 1)
                if 0 < b < L and i == 5 or b == L and i == 4:
                    copy_rden(b - 1, 0)
                if 0 < b < L and i == 6:
                    copy_rden(b - 1, 1)

        @block.vector
        def _(dve):
            def channel_stats(b, f):
                if b > 0:
                    dve.wait_ge(chan_ready, b)
                dve.bn_stats(bn[:, f, :], x_sb[:, b, BANK * f:BANK * (f + 1)]).then_inc(bn_ready, 1)

            def channel_means(b):
                dve.wait_ge(bn_ready, HALVES * (b + 1))
                if b > 0:
                    dve.wait_ge(gmean_psum, b)
                    dve.wait_ge(cvar_ready, b)
                dve.bn_aggr(chan[:, :], bn[:, :, :].rearrange("p a b -> p (a b)")).then_inc(chan_ready, 1)

            def channel_vars(b):
                dve.wait_ge(gmean_psum, b + 1)
                if b > 0:
                    dve.wait_ge(gms_ready, b)
                dve.tensor_copy(gmean[:, :], BC[:, 0:1]).then_inc(gmean_ready, 1)
                dve.wait_ge(gmean_ready, b + 1)
                dve.tensor_tensor(dmean[:, :], chan[:, 0:1], gmean[:, :], ALU.subtract).then_inc(dmean_ready, 1)
                dve.wait_ge(dmean_ready, b + 1)
                dve.scalar_tensor_tensor(cvar[:, :], dmean[:, :], dmean[:, 0:1], chan[:, 1:2], ALU.mult, ALU.add)\
                   .then_inc(cvar_ready, 1)

            def group_var(b):
                dve.wait_ge(gvar_psum, b + 1)
                dve.tensor_scalar(gvar[:, :], BC[:, 2:3], EPS, None, ALU.add).then_inc(gvar_ready, 1)

            def shift(b):
                dve.wait_ge(gscale_ready, b + 1)
                dve.tensor_tensor(gms[:, :], gmean[:, :], gscale[:, :], ALU.mult).then_inc(gms_ready, 1)
                dve.wait_ge(gms_ready, b + 1)
                dve.tensor_tensor(gshift[:, :], cols[:, GNB:GNB + 1], gms[:, :], ALU.subtract).then_inc(gshift_ready, 1)

            def normalize(b, f0, f1):
                dve.wait_ge(gshift_ready, b + 1)
                if b > 0:
                    dve.wait_ge(v_psum, VP * b)
                cs = slice(BANK * f0, BANK * f1)
                dve.tensor_scalar(h[:, cs], x_sb[:, b, cs], gscale[:, :], gshift[:, :], ALU.mult, ALU.add)\
                   .then_inc(h_ready, f1 - f0)

            def split_k(b):
                for f in range(HALVES):
                    dve.wait_ge(k_hi_ready, HALVES * b + f + 1)
                    cs = slice(BANK * f, BANK * (f + 1))
                    dve.scalar_tensor_tensor(qk_lo[:, 1, cs], S[:, 0, cs], cols[:, KB:KB + 1], qk_hi[:, 1, cs].bitcast(F32),
                                             ALU.add, ALU.subtract).then_inc(k_lo_ready, 1)

            def split_q(b):
                for f in range(HALVES):
                    dve.wait_ge(q_hi_ready, 2 * b + f + 1)
                    cs = slice(BANK * f, BANK * (f + 1))
                    dve.scalar_tensor_tensor(qk_lo[:, 0, cs], S[:, 1, cs], qb_scaled[:, :], qk_hi[:, 0, cs].bitcast(F32),
                                             ALU.add, ALU.subtract).then_inc(q_lo_ready, 1)

            def row_max(c):
                i = c % CH
                dve.wait_ge(scores_psum, c + 1)
                dve.tensor_reduce(negmax[:, i:i + 1], S[:, c % 2, :], AX.X, ALU.max, negate=True)\
                   .then_inc(negmax_ready, 1)

            def transpose_blocks(c):
                b, i = c // CH, c % CH
                dve.wait_ge(probs_ready, c + 1)
                if i == 0 and b > 1:
                    for a in range(NQ):
                        dve.wait_ge(moved[a], MOVED * (b - 1))
                dve.transpose(blocks[b % 2][:, :, :, i, :].rearrange("p j t q -> p t j q"),
                              probs[:, c % 2, :].rearrange("p (t j q) -> p t j q", t=KT, j=NQ)).then_inc(blocks_ready, 1)

            def invert_denominators(c):
                b, i = c // CH, c % CH
                if i % GC == GC - 1:
                    g = i // GC
                    if b > 1:
                        dve.wait_ge(bc_psum, 2 * (b - 2) + g + 1)
                    dve.wait_ge(probs_ready, c + 1)
                    dve.reciprocal(rden[:, b % 2, GC * g:GC * (g + 1)], den[:, GC * g:GC * (g + 1)])\
                       .then_inc(rden_ready, 1)

            def divide(b, half):
                dve.wait_ge(part_done, CH * b + 4 * (half + 1))
                dve.wait_ge(bc_ready, 2 * (b + 1))
                a = slice(2 * half, 2 * half + 2)
                by_rden = rden_bc[:, :].rearrange("p (c a q) -> p c a q", c=CH, a=NQ)[:, :, a, :]
                dve.tensor_tensor(by_rden, ACC[:, a, :].rearrange("p a (c q) -> p c a q", c=CH), by_rden, ALU.mult)\
                   .then_inc(normed_ready, 1)

            def split_v(b, p):
                dve.wait_ge(v_hi_ready, VP * b + p + 1)
                ts = slice(VT * p, VT * (p + 1))
                hi, lo = (vL_hi, vL_lo) if b == L else (v_hi[:, b % 2], v_lo[:, b % 2])
                dve.tensor_tensor(lo[:, ts, :], VT_PS[:, :].rearrange("p (t c) -> p t c", t=VT),
                                  hi[:, ts, :].bitcast(F32), ALU.subtract).then_inc(v_lo_ready, 1)

            def split_pairs(c):
                r, d = (c - DIRECT) // 2, c % 2
                for f in range(2):
                    dve.wait_ge(pair_hi_ready, 2 * (c - DIRECT) + f + 1)
                    if r > 1:
                        dve.wait_ge(pair_done, r - 1)
                    ts = slice(PT * f, PT * (f + 1))
                    dve.tensor_tensor(pair_lo[:, r % 2, ts, d, :], S[:, c % 2, BANK * f:BANK * (f + 1)]
                                      .rearrange("p (t q) -> p t q", t=PT),
                                      pair_hi[:, r % 2, ts, d, :].bitcast(F32), ALU.subtract).then_inc(pair_lo_ready, 1)

            def finish_pair(r):
                dve.wait_ge(bc_ready, 2 * L + r // 2 + 1)
                dve.wait_ge(pair_done, max(r + 1, 2))
                cs = slice(PN * r, PN * (r + 1))
                dve.tensor_tensor(rdenL_bc[:, cs], pair_out[r], rdenL_bc[:, cs], ALU.mult).then_inc(pair_normed, 1)
                dve.wait_ge(pair_normed, r + 1)
                dve.wait_ge(resid_ready, B)
                dve.tensor_tensor(x_sb[:, L, cs], rdenL_bc[:, cs], x_sb[:, L, cs], ALU.add).then_inc(pair_out_ready, 1)

            dve.memset(minus_half[:, :], -0.5).then_inc(half_ready, 1)
            for f in range(HALVES):
                dve.wait_ge(x0_loaded[f], 16)
                channel_stats(0, f)
            channel_means(0)
            dve.wait_ge(cols_loaded, 16)
            dve.tensor_scalar(qb_scaled[:, :], cols[:, QB:QB + 1], SCALE, None, ALU.mult).then_inc(qbs_ready, 1)
            channel_vars(0)
            group_var(0)
            for w, scale in ((QW, SCALE), (KW, 1.0)):
                dve.wait_ge(wqk_hi_ready, w + 1)
                dve.scalar_tensor_tensor(wqk_lo[:, w, :], w_in[:, w, :], scale, wqk_hi[:, w, :].bitcast(F32),
                                         ALU.mult, ALU.subtract).then_inc(wqk_lo_ready, 1)
            shift(0)
            for f in range(HALVES):
                normalize(0, f, f + 1)
            for f in range(HALVES):
                dve.wait_ge(h_ready, f + 1)
                dve.wait_ge(h_hi_ready, f + 1)
                cs = slice(BANK * f, BANK * (f + 1))
                dve.tensor_tensor(h_lo[:, cs], h[:, cs], h_hi[:, cs].bitcast(F32), ALU.subtract).then_inc(h_lo_ready, 1)
            dve.wait_ge(pv_psum, 1)
            dve.tensor_copy(wpv[:, :], BC[:, 0:P]).then_inc(wpv_ready, 1)
            dve.tensor_tensor(out_bias[:, :], BC[:, P:P + 1], cols[:, PB:PB + 1], ALU.add).then_inc(bias_ready, 1)
            split_k(0)
            split_q(0)

            for c in range(STEPS + 1):
                b, i = c // CH, c % CH
                if b < L and i == 0:
                    dve.wait_ge(xs_loaded, 16)
                    channel_stats(b + 1, 0)
                if b < L and i == 3:
                    channel_vars(b + 1)
                if b == L and i == 3:
                    split_v(b, 1)
                if b < L and i == 6:
                    shift(b + 1)
                    if b > 0:
                        normalize(b + 1, 0, HALVES)
                if 0 < b < B and i == 0:
                    split_k(b)
                    split_q(b)
                    transpose_blocks(c - 1)
                    invert_denominators(c - 1)
                if c == DIRECT + 7:
                    finish_pair(0)
                    finish_pair(1)
                if c > DIRECT:
                    invert_denominators(c - 1)
                if c < STEPS:
                    row_max(c)
                m = c - LAG - 4
                if m >= 0 and m % 4 == 0 and m < CH * (L - 1):
                    divide(m // CH, m % CH // 4)
                if b < L and i == 1:
                    channel_stats(b + 1, 1)
                    channel_means(b + 1)
                if b == 0 and i == 7 or 0 < b < L and i == 6:
                    split_v(b, 1)
                if 0 < c <= DIRECT and i > 0:
                    transpose_blocks(c - 1)
                    invert_denominators(c - 1)
                if c > DIRECT:
                    split_pairs(c - 1)
                if b < L and i == 3:
                    group_var(b + 1)
                if b == 0 and i == 4 or 0 < b < L and i == 3 or b == L and i == 0:
                    split_v(b, 0)
                if c == DIRECT + 7:
                    divide(L - 1, 0)
            divide(L - 1, 1)
            finish_pair(2)
            finish_pair(3)

        @block.gpsimd
        def _(pool):
            def group_scale(b):
                pool.wait_ge(gvar_ready, b + 1)
                if b > 0:
                    pool.wait_ge(h_ready, HALVES * b)
                    pool.wait_ge(h_hi_ready, HALVES * b)
                pool.tensor_tensor(rstd[:, :], gvar[:, :], minus_half[:, :], ALU.pow).then_inc(rstd_ready, 1)
                pool.wait_ge(rstd_ready, b + 1)
                pool.tensor_tensor(gscale[:, :], rstd[:, :], cols[:, GNW:GNW + 1], ALU.mult).then_inc(gscale_ready, 1)

            def normalize(b):
                pool.wait_ge(gshift_ready, b + 1)
                pool.wait_ge(v_psum, VP * b)
                pool.tensor_scalar(h[:, :], x_sb[:, b, :], gscale[:, :], gshift[:, :], ALU.mult, ALU.add)\
                    .then_inc(h_ready, HALVES)

            def split_h(b):
                pool.wait_ge(h_ready, HALVES * (b + 1))
                pool.wait_ge(h_hi_ready, HALVES * (b + 1))
                pool.wait_ge(q_psum, HALVES * b)
                pool.tensor_tensor(h_lo[:, :], h[:, :], h_hi[:, :].bitcast(F32), ALU.subtract)\
                    .then_inc(h_lo_ready, HALVES)

            def split_probs(m):
                n = m % CH
                a, half = n // 2, n % 2
                pool.wait_ge(p_hi_ready, m + 1)
                pool.tensor_tensor(p_lo[:, m % RING], pT[:, a, PT * half:PT * (half + 1), :],
                                   p_hi[:, m % RING].bitcast(F32), ALU.subtract).then_inc(p_lo_ready, 1)

            def add_residual(b, half):
                pool.wait_ge(normed_ready, 2 * b + half + 1)
                pool.wait_ge(resid_ready, b + 1)
                xs, normed = (v.rearrange("p (c h r) -> p c h r", c=CH, h=2)[:, :, half, :]
                              for v in (x_sb[:, b, :], rden_bc[:, :]))
                pool.tensor_tensor(xs, normed, xs, ALU.add)\
                    .then_inc(out_ready, 1)

            pool.memset(ident[:, :], 0.0).then_inc(gm_ready, 1)
            pool.wait_ge(gm_ready, 1)
            pool.affine_select(out=ident[:, :], in_=ident[:, :], compare_op=ALU.not_equal, fill=1.0, base=0,
                               pattern=[[-1, P]], channel_multiplier=1).then_inc(ident_ready, 1)
            gm = group_mean[:, :].rearrange("p (g c) -> p g c", g=GROUPS)
            pool.memset(group_mean[:, :], 1.0 / CPG).then_inc(gm_ready, 1)
            pool.wait_ge(gm_ready, 2)
            pool.affine_select(out=gm, in_=gm, compare_op=ALU.is_ge, fill=0.0, base=0,
                               pattern=[[-CPG, GROUPS], [0, CPG]], channel_multiplier=1).then_inc(ident_ready, 1)
            pool.wait_ge(ident_ready, 2)
            pool.affine_select(out=gm, in_=gm, compare_op=ALU.is_ge, fill=0.0, base=CPG - 1,
                               pattern=[[CPG, GROUPS], [0, CPG]], channel_multiplier=-1).then_inc(gm_ready, 1)
            pool.wait_ge(half_ready, 1)
            pool.wait_ge(cols_loaded, 16)
            group_scale(0)

            for c in range(STEPS + 1):
                b, i = c // CH, c % CH
                if b < L and i == 3:
                    group_scale(b + 1)
                if b == 0 and i == 5:
                    normalize(b + 1)
                if b < L and i == 5:
                    split_h(b + 1)
                m = c - LAG - 4
                if m >= 0 and m % 4 == 0 and m < CH * (L - 1):
                    add_residual(m // CH, m % CH // 4)
                for m in parts_split(c):
                    split_probs(m)
                if c == DIRECT + 7:
                    add_residual(L - 1, 0)
            add_residual(L - 1, 1)


def kernel(x, L0_conv_gn_w, L0_conv_gn_b, L0_conv_qw, L0_conv_qb, L0_conv_kw, L0_conv_kb,
           L0_conv_vw, L0_conv_vb, L0_conv_pw, L0_conv_pb):
    import numpy as np
    import concourse.bacc as bacc
    from concourse.bass_utils import run_bass_kernel_spmd

    B, C, H, W = x.shape
    given = {
        "x": np.asarray(x).reshape(B, C, H * W),
        "vectors": np.stack([L0_conv_gn_w, L0_conv_gn_b, L0_conv_qb, L0_conv_kb, L0_conv_vb, L0_conv_pb], axis=1),
        "weights": np.stack([np.transpose(L0_conv_qw), np.transpose(L0_conv_kw), np.transpose(L0_conv_pw), L0_conv_vw]),
    }
    arrays = {name: np.ascontiguousarray(a) for name, a in given.items()}
    nc = bacc.Bacc("TRN2", target_bir_lowering=False, num_devices=1)
    ins = {n: nc.dram_tensor(n, a.shape, mybir.dt.from_np(a.dtype), kind="ExternalInput").ap()
           for n, a in arrays.items()}
    out = nc.dram_tensor("out", arrays["x"].shape, F32, kind="ExternalOutput").ap()
    build(nc, **ins, out=out)
    got = run_bass_kernel_spmd(nc, [arrays], core_ids=[0])
    return got.results[0]["out"].reshape(B, C, H, W)
```
